# Optimizing a Trainium2 kernel written in Bass

```python
import numpy as np
import jax
import jax.numpy as jnp

def _softmax(x, axis=-1):
    return jax.nn.softmax(x, axis=axis)

def _gelu(x):
    return jax.nn.gelu(x, approximate=True)

def _silu(x):
    return jax.nn.silu(x)

def _sigmoid(x):
    return jax.nn.sigmoid(x)

def _layernorm(x, axis=-1, eps=1e-05):
    m = jnp.mean(x, axis=axis, keepdims=True)
    v = jnp.var(x, axis=axis, keepdims=True)
    return (x - m) / jnp.sqrt(v + eps)

def _scatter_add(tgt, idx, src, axis=0):
    return tgt.at[idx].add(src)

def _segment_sum(src, seg, n):
    return jax.ops.segment_sum(src, seg, n)
kernel_name = 'mk_xattn_ffn_d1_seqx_r2_b17d90'

def setup_inputs(seed: int=0):
    np.random.seed(seed)
    _w = jnp.asarray

    def _rec_inputs():
        import jax
        import jax.numpy as jnp
        _rk = jax.random.key(seed)
        x = 7.22e-05 + 1 * jax.random.normal(jax.random.fold_in(_rk, 1), (64, 256, 1024), jnp.float32)
        _lenS = 256 - jax.random.randint(jax.random.fold_in(_rk, 7), (64,), 0, max(1, 256 // 4) + 1, jnp.int32)
        _lenS2 = 256 - jax.random.randint(jax.random.fold_in(_rk, 8), (64,), 0, max(1, 256 // 4) + 1, jnp.int32)
        _ctx_512P = jax.random.normal(jax.random.fold_in(_rk, 11), (64, 16, 256), jnp.float32)
        _ctx_512c = jax.random.dirichlet(jax.random.fold_in(_rk, 511), 0.3 * jnp.ones((16,), jnp.float32), (64, 256))
        _ctx_512t = jnp.einsum('bsk,bkd->bsd', _ctx_512c, _ctx_512P)
        _ctx_512t = _ctx_512t * jax.lax.rsqrt(jnp.mean(jnp.square(_ctx_512t)) + 1e-12) * 0.953939
        ctx_512 = -0.000514642 + 1.00011 * (_ctx_512t + 0.3 * jax.random.normal(jax.random.fold_in(_rk, 611), (64, 256, 256), jnp.float32))
        return (x, ctx_512)
    x, ctx_512 = _rec_inputs()

    def _L0_xattn_setup():
        import jax, jax.numpy as jnp
        import numpy as np
        import math
        NUM_Q_HEADS = 32
        NUM_KV_HEADS = 8
        key = jax.random.key(seed)
        k1, k2, k3 = jax.random.split(key, 3)
        B, S, E = (2, 1024, 1024)
        kv_E = NUM_KV_HEADS * (E // NUM_Q_HEADS)
        q = jax.random.normal(k1, (B, S, E), dtype=jnp.float32)
        k = jax.random.normal(k2, (B, S, kv_E), dtype=jnp.float32)
        v = jax.random.normal(k3, (B, S, kv_E), dtype=jnp.float32)
        return {'q': q, 'k': k, 'v': v}
    _L0_xattn_all = _L0_xattn_setup()
    _L0_xattn_in = {k: v for k, v in _L0_xattn_all.items() if k in ()}
    del _L0_xattn_all

    def _L0_ffn_setup():
        import jax, jax.numpy as jnp
        import numpy as np
        H = 1024
        I = 704
        E = 8
        K = 2
        B, S = (4, 1024)

        def _moe(x, router_w, w1, w2):
            b, s, h = x.shape
            xf = x.reshape(-1, h)
            T = xf.shape[0]
            logits = xf @ router_w.T
            topk_vals, topk_idx = jax.lax.top_k(logits, K)
            topk_w = jax.nn.softmax(topk_vals, axis=-1)
            exp_id = topk_idx.reshape(-1)
            exp_w = topk_w.reshape(-1)
            order = jnp.argsort(exp_id)
            x_sorted = xf[order // K]
            counts = jnp.bincount(exp_id, length=E).astype(jnp.int32)
            y1 = jax.lax.ragged_dot(x_sorted, jnp.swapaxes(w1, 1, 2), counts)
            gate, up = jnp.split(y1, 2, axis=-1)
            y_act = jax.nn.silu(gate) * up
            y2 = jax.lax.ragged_dot(y_act, jnp.swapaxes(w2, 1, 2), counts)
            inv = jnp.argsort(order)
            y_pairs = y2[inv] * exp_w[:, None]
            y = y_pairs.reshape(T, K, h).sum(axis=1)
            return y.reshape(b, s, h)
        key = jax.random.key(seed)
        k1, k2, k3, k4 = jax.random.split(key, 4)
        x = jax.random.normal(k1, (B, S, H), dtype=jnp.float32)
        router_w = jax.random.normal(k2, (E, H), dtype=jnp.float32) * 0.02
        w1 = jax.random.normal(k3, (E, 2 * I, H), dtype=jnp.float32) * 0.02
        w2 = jax.random.normal(k4, (E, H, I), dtype=jnp.float32) * 0.02
        return {'x': x, 'router_w': router_w, 'w1': w1, 'w2': w2}
    _L0_ffn_all = _L0_ffn_setup()
    _L0_ffn_in = {k: v for k, v in _L0_ffn_all.items() if k in ('router_w', 'w1', 'w2')}
    del _L0_ffn_all
    return {'x': x, 'ctx_512': ctx_512, 'L0_ffn_router_w': _L0_ffn_in['router_w'], 'L0_ffn_w1': _L0_ffn_in['w1'], 'L0_ffn_w2': _L0_ffn_in['w2']}

def reference(x, ctx_512, L0_ffn_router_w, L0_ffn_w1, L0_ffn_w2):
    import jax
    import jax.numpy as jnp

    def _L0_xattn_ref(q, k, v):
        import jax, jax.numpy as jnp
        import numpy as np
        import math
        NUM_Q_HEADS = 32
        NUM_KV_HEADS = 8
        B, S, E = q.shape
        H, KV = (NUM_Q_HEADS, NUM_KV_HEADS)
        D = E // H
        G = H // KV
        scale = math.sqrt(D)
        qh = q.reshape(B, S, KV, G, D).transpose(0, 2, 3, 1, 4)
        kh = k.reshape(B, S, KV, D).transpose(0, 2, 1, 3)
        vh = v.reshape(B, S, KV, D).transpose(0, 2, 1, 3)
        scores = jnp.einsum('bkgsd,bktd->bkgst', qh, kh) / scale
        weights = jax.nn.softmax(scores, axis=-1)
        out = jnp.einsum('bkgst,bktd->bkgsd', weights, vh)
        return out.transpose(0, 3, 1, 2, 4).reshape(B, S, E)

    def _L0_ffn_ref(x, router_w, w1, w2):
        import jax, jax.numpy as jnp
        import numpy as np
        H = 1024
        I = 704
        E = 8
        K = 2
        B, S = (4, 1024)

        def _moe(x, router_w, w1, w2):
            b, s, h = x.shape
            xf = x.reshape(-1, h)
            T = xf.shape[0]
            logits = xf @ router_w.T
            topk_vals, topk_idx = jax.lax.top_k(logits, K)
            topk_w = jax.nn.softmax(topk_vals, axis=-1)
            exp_id = topk_idx.reshape(-1)
            exp_w = topk_w.reshape(-1)
            order = jnp.argsort(exp_id)
            x_sorted = xf[order // K]
            counts = jnp.bincount(exp_id, length=E).astype(jnp.int32)
            y1 = jax.lax.ragged_dot(x_sorted, jnp.swapaxes(w1, 1, 2), counts)
            gate, up = jnp.split(y1, 2, axis=-1)
            y_act = jax.nn.silu(gate) * up
            y2 = jax.lax.ragged_dot(y_act, jnp.swapaxes(w2, 1, 2), counts)
            inv = jnp.argsort(order)
            y_pairs = y2[inv] * exp_w[:, None]
            y = y_pairs.reshape(T, K, h).sum(axis=1)
            return y.reshape(b, s, h)
        return _moe(x, router_w, w1, w2)
    x = x + _L0_xattn_ref(_layernorm(x, axis=-1), ctx_512, ctx_512)
    x = x + _L0_ffn_ref(_layernorm(x, axis=-1), L0_ffn_router_w, L0_ffn_w1, L0_ffn_w2)
    return x

_drawn_inputs = setup_inputs


def setup_inputs(seed=0):
    import zlib

    import numpy as np

    out = dict(_drawn_inputs(seed))
    spreads = {}
    factors = {}
    for name, (base, spread) in spreads.items():
        noise = np.random.default_rng([zlib.crc32(name.encode()), seed]).standard_normal(out[name].shape)
        drawn = base * np.exp(spread * noise) if base else spread * noise
        out[name] = jnp.asarray(drawn.astype(out[name].dtype))
    for name, factor in factors.items():
        out[name] = (out[name] * factor).astype(out[name].dtype)
    return out
```

```python
from contextlib import ExitStack

import concourse.bass as bass
from concourse import mybir

P = 128
ALU = mybir.AluOpType
ACT = mybir.ActivationFunctionType
AX = mybir.AxisListType
F32 = mybir.dt.float32
F16 = mybir.dt.float16
I32 = mybir.dt.int32
U32 = mybir.dt.uint32
RMAX = bass.bass_isa.ReduceOp.max
EPS = 1e-5
EXPONENT = 0x7F800000
KV = 8
G = 4
D = 32
BLOCK = 512


def at_least(eng, sem, value):
    if not isinstance(value, int) or value > 0:
        eng.wait_ge(sem, value)


def settle(eng, passed):
    eng.sem_inc(passed, 1)


def prepare_weights(nc, w1, w2, router_w, w1_parts, w2_parts, scales, slots_init, router_parts, router_scale,
                    ident, tokens):
    E, F2, H = w1.shape
    I = F2 // 2
    FT = F2 // P
    HT = H // P
    FULL = I // P
    HALF = I - FULL * P
    IT = FULL + 1
    CH = FT + IT
    GROUPS = 2 * CH
    SLOTS = 6
    BANKS = 4
    LOADS = FT + 3
    assert HALF == P // 2 and FT == 2 * FULL + 1 and E % 2 == 0 and HT == 8
    w2_rows = w2.rearrange("e (t p) i -> e p t i", p=P)

    with ExitStack() as ctx:
        def sb(name, shape, dt):
            return ctx.enter_context(nc.sbuf_tensor(name, shape, dt))

        def sem(name):
            return ctx.enter_context(nc.semaphore(name))

        w1_in = sb("w1_in", [P, 2, FT, H], F32)
        w2_in = sb("w2_in", [P, 2, HT, IT * P], F32)
        parts = sb("w_parts", [P, SLOTS, 2 * H], F16)
        tile_max = sb("w_tile_max", [P, FT + HT], F32)
        part_max = sb("w_part_max", [P, 2], F32)
        all_max = sb("w_all_max", [P, 2], F32)
        guarded = sb("w_guarded", [P, 2], F32)
        pow2 = sb("w_pow2", [P, 2], F32)
        rec2 = sb("w_rec2", [P, 2], F32)
        inv = sb("w_inv", [P, 2, 2], F32)
        pow2sq = sb("w_pow2sq", [P, 1], F32)
        const32 = sb("w_const32", [P, 1], F32)
        sc = sb("w_scales", [P, 4], F32)
        n_slots = slots_init.shape[0] // P
        empty = sb("w_empty", [P, n_slots, 2], U32)
        r_in = sb("r_in", [E, H], F32)
        r_scaled = sb("r_scaled", [P, HT, E], F32)
        r_max = sb("r_max", [P, 1], F32)
        r_all = sb("r_all", [P, 1], F32)
        r_guard = sb("r_guard", [P, 1], F32)
        r_pow2 = sb("r_pow2", [P, 1], F32)
        r_rec = sb("r_rec", [P, 1], F32)
        r_inv = sb("r_inv", [P, 1], F32)
        banks = ctx.enter_context(nc.psum_tensor("w_banks", [P, BANKS, 4, P], F32))
        r_bank = ctx.enter_context(nc.psum_tensor("r_bank", [P, HT, E], F32))

        w_loaded = [sem("w_loaded0"), sem("w_loaded1")]
        tiles_maxed = sem("w_tiles_maxed")
        maxed = sem("w_maxed")
        reduced = sem("w_reduced")
        chain = sem("w_chain")
        scaled = sem("w_scaled")
        transposed = sem("w_transposed")
        high = sem("w_high")
        low = sem("w_low")
        stored = [sem(f"w_stored{i}") for i in range(SLOTS)]
        scales_stored = sem("w_scales_stored")
        empty_made = sem("w_empty_made")
        empty_stored = sem("w_empty_stored")
        passed = sem("w_passed")
        const_made = sem("w_const_made")
        r_loaded = sem("r_loaded")
        r_transposed = sem("r_transposed")
        r_reduced = sem("r_reduced")
        r_chain = sem("r_chain")
        USES = [-(-(CH - s) // SLOTS) for s in range(SLOTS)]
        CHAIN = 6
        block = ctx.enter_context(nc.Block())

        def over_experts(eng, body):
            body(0, 0)
            body(1, 1)
            with eng.Fori(1, E // 2) as r:
                body(r * 2, 0)
                body(r * 2 + 1, 1)

        def wait_loaded(eng, e, par):
            eng.wait_ge(w_loaded[par], (e - par) * (8 * LOADS) + 16 * LOADS)

        def bank(par, g):
            return banks[:, (2 * par + g) % BANKS, :, :]

        def dest(c, half, part):
            v = parts[:, c % SLOTS, :]
            if c < FT:
                return v.rearrange("p (t s f) -> p t s f", s=2, f=P)[:, half * 4:half * 4 + 4, part, :]
            return v.rearrange("p (s t f) -> p s t f", s=2, f=P)[:, part, half * 4:half * 4 + 4, :]

        def inv_of(par, c):
            return inv[:, par, 0:1] if c < FT else inv[:, par, 1:2]

        @block.sync
        def _(sp):
            sp.dma_start(r_in[:, :], router_w).then_inc(r_loaded, 16)

            def load(e, par):
                at_least(sp, transposed, (e - 1) * GROUPS)
                for j in range(2 * FULL):
                    row = (j // 2) * P + (j % 2) * I
                    sp.dma_start(w1_in[:, par, j, :], w1[bass.ds(e, 1), row:row + P, :]
                                 .rearrange("a p h -> (a p) h")).then_inc(w_loaded[par], 16)
                for at, row in ((0, FULL * P), (HALF, I + FULL * P)):
                    sp.dma_start(w1_in[at:at + HALF, par, FT - 1, :], w1[bass.ds(e, 1), row:row + HALF, :]
                                 .rearrange("a p h -> (a p) h")).then_inc(w_loaded[par], 16)
                sp.dma_start(w2_in[:, par, :, 0:I], w2_rows[bass.ds(e, 1), :, :, :]
                             .rearrange("a p t i -> (a p) t i")).then_inc(w_loaded[par], 16)
                sp.dma_start(w2_in[:, par, :, I:IT * P], w2_rows[bass.ds(e, 1), :, :, FULL * P:I]
                             .rearrange("a p t i -> (a p) t i")).then_inc(w_loaded[par], 16)

            def store(e, par):
                sp.wait_ge(scaled, e + 1)
                sp.dma_start(scales[bass.ds(e * P, P), :], sc[:, :]).then_inc(scales_stored, 16)
                for c in range(CH):
                    sp.wait_ge(low, e * GROUPS + (2 * c + 2))
                    to = w1_parts[bass.ds(e * (FT * P) + c * P, P), :] if c < FT else \
                        w2_parts[bass.ds(e * (IT * P) + (c - FT) * P, P), :]
                    sp.dma_start(to, parts[:, c % SLOTS, :]).then_inc(stored[c % SLOTS], 16)

            load(0, 0)
            load(1, 1)
            sp.wait_ge(empty_made, 2)
            sp.dma_start(slots_init.rearrange("(p n) c -> p n c", p=P), empty[:, :, :]).then_inc(empty_stored, 16)
            store(0, 0)
            with sp.Fori(1, E // 2) as r:
                load(r * 2, 0)
                store(r * 2 - 1, 1)
                load(r * 2 + 1, 1)
                store(r * 2, 0)
            store(E - 1, 1)
            sp.wait_ge(scales_stored, 16 * E)
            sp.wait_ge(empty_stored, 16)
            for s in range(SLOTS):
                sp.wait_ge(stored[s], 16 * E * USES[s])

        @block.tensor
        def _(pe):
            pe.wait_ge(r_loaded, 16)
            for t in range(HT):
                last = pe.transpose(r_bank[:, t, :], r_in[:, t * P:(t + 1) * P], ident[0:E, 0:E])
            last.then_inc(r_transposed, 1)

            def transposes(e, par):
                wait_loaded(pe, e, par)
                for c in range(CH):
                    for half in range(2):
                        g = 2 * c + half
                        at_least(pe, low, e * GROUPS + (g - BANKS + 1))
                        for q in range(4):
                            t = half * 4 + q
                            src = w1_in[:, par, c, t * P:(t + 1) * P] if c < FT else \
                                w2_in[:, par, t, (c - FT) * P:(c - FT + 1) * P]
                            last = pe.transpose(bank(par, g)[:, q, :], src, ident[:, :])
                        last.then_inc(transposed, 1)

            over_experts(pe, transposes)

        @block.scalar
        def _(act):
            def highs(e, par):
                act.wait_ge(scaled, e + 1)
                for c in range(CH):
                    s = c % SLOTS
                    at_least(act, stored[s], e * (16 * USES[s]) + 16 * (c // SLOTS))
                    for half in range(2):
                        g = 2 * c + half
                        act.wait_ge(transposed, e * GROUPS + (g + 1))
                        act.activation(dest(c, half, 0), bank(par, g), ACT.Copy,
                                       scale=inv_of(par, c)).then_inc(high, 1)

            over_experts(act, highs)

        @block.gpsimd
        def _(pool):
            pool.memset(empty[:, :, 0:1], tokens).then_inc(empty_made, 1)
            pool.memset(empty[:, :, 1:2], 0).then_inc(empty_made, 1)
            pool.wait_ge(r_chain, 1)
            pool.partition_all_reduce(r_all[:, :], r_max[:, :], P, RMAX).then_inc(r_reduced, 1)

            def over_partitions(e, par):
                pool.wait_ge(maxed, e + 1)
                at_least(pool, scaled, e)
                settle(pool, passed)
                pool.partition_all_reduce(all_max[:, :], part_max[:, :], P, RMAX).then_inc(reduced, 1)

            over_experts(pool, over_partitions)

        @block.vector
        def _(dve):
            dve.memset(const32[:, :], 32.0).then_inc(const_made, 1)
            dve.wait_ge(const_made, 1)
            dve.wait_ge(r_transposed, 1)
            dve.reduce_max(r_max[:, :], r_bank[:, :, :], AX.XY, apply_absolute_value=True).then_inc(r_chain, 1)
            dve.wait_ge(r_reduced, 1)
            dve.tensor_scalar(r_guard[:, :], r_all[:, :], 1e-30, None, ALU.max).then_inc(r_chain, 1)
            dve.wait_ge(r_chain, 2)
            dve.tensor_single_scalar(r_pow2[:, :].bitcast(I32), r_guard[:, :].bitcast(I32), EXPONENT,
                                     ALU.bitwise_and).then_inc(r_chain, 1)
            dve.wait_ge(r_chain, 3)
            dve.reciprocal(r_rec[:, :], r_pow2[:, :]).then_inc(r_chain, 1)
            dve.tensor_scalar(router_scale[:, :], r_pow2[:, :], 0.125, None, ALU.mult).then_inc(r_chain, 1)
            dve.wait_ge(r_chain, 5)
            dve.tensor_scalar(r_inv[:, :], r_rec[:, :], 8.0, None, ALU.mult).then_inc(r_chain, 1)
            dve.wait_ge(r_chain, 6)
            dve.tensor_scalar(r_scaled[:, :, :], r_bank[:, :, :], r_inv[:, 0:1], None, ALU.mult).then_inc(r_chain, 1)
            dve.wait_ge(r_chain, 7)
            dve.tensor_copy(router_parts[:, :, 0, :], r_scaled[:, :, :]).then_inc(r_chain, 1)
            dve.wait_ge(r_chain, 8)
            dve.tensor_tensor(router_parts[:, :, 1, :], r_scaled[:, :, :], router_parts[:, :, 0, :],
                              ALU.subtract).then_inc(r_chain, 1)

            def expert(e, par):
                wait_loaded(dve, e, par)
                dve.reduce_max(tile_max[:, 0:FT], w1_in[:, par, :, :], AX.X,
                               apply_absolute_value=True).then_inc(tiles_maxed, 1)
                dve.reduce_max(tile_max[:, FT:FT + HT], w2_in[:, par, :, 0:I], AX.X,
                               apply_absolute_value=True).then_inc(tiles_maxed, 1)
                dve.wait_ge(tiles_maxed, e * 2 + 2)
                dve.reduce_max(part_max[:, 0:1], tile_max[:, 0:FT], AX.X)
                dve.reduce_max(part_max[:, 1:2], tile_max[:, FT:FT + HT], AX.X).then_inc(maxed, 1)
                dve.wait_ge(reduced, e + 1)
                dve.tensor_scalar(guarded[:, :], all_max[:, :], 1e-30, None, ALU.max).then_inc(chain, 1)
                dve.wait_ge(chain, e * CHAIN + 1)
                dve.tensor_single_scalar(pow2[:, :].bitcast(I32), guarded[:, :].bitcast(I32), EXPONENT,
                                         ALU.bitwise_and).then_inc(chain, 1)
                dve.wait_ge(chain, e * CHAIN + 2)
                dve.reciprocal(rec2[:, :], pow2[:, :]).then_inc(chain, 1)
                dve.tensor_tensor(pow2sq[:, :], pow2[:, 0:1], pow2[:, 0:1], ALU.mult).then_inc(chain, 1)
                dve.wait_ge(chain, e * CHAIN + 4)
                at_least(dve, scales_stored, e * 16)
                dve.tensor_scalar(inv[:, par, :], rec2[:, :], 8.0, None, ALU.mult).then_inc(chain, 1)
                dve.tensor_scalar(sc[:, 0:1], pow2[:, 0:1], 0.125, None, ALU.mult)
                dve.tensor_scalar(sc[:, 1:2], rec2[:, 0:1], 2.0 ** -11, None, ALU.mult)
                dve.tensor_scalar(sc[:, 3:4], rec2[:, 0:1], 1.0, None, ALU.mult)
                dve.scalar_tensor_tensor(out=sc[:, 2:3], in0=pow2sq[:, :], scalar=pow2[:, 1:2],
                                         in1=const32[:, :], op0=ALU.mult, op1=ALU.mult)\
                   .then_inc(chain, 1)
                dve.wait_ge(chain, e * CHAIN + 6)
                dve.tensor_copy(r_guard[:, :], sc[:, 2:3]).then_inc(scaled, 1)
                for c in range(CH):
                    for half in range(2):
                        g = 2 * c + half
                        dve.wait_ge(high, e * GROUPS + (g + 1))
                        dve.scalar_tensor_tensor(out=dest(c, half, 1), in0=bank(par, g), scalar=inv_of(par, c),
                                                 in1=dest(c, half, 0), op0=ALU.mult, op1=ALU.subtract)\
                           .then_inc(low, 1)

            over_experts(dve, expert)


def make_constants(nc, ident, ident16, strict, ones16, expert_order, tok, next_slot, capacity):
    E = expert_order.shape[2]
    with ExitStack() as ctx:
        def sem(name):
            return ctx.enter_context(nc.semaphore(name))

        iota_i = ctx.enter_context(nc.sbuf_tensor("c_iota", [P, 2 * E], I32))
        iota_e = ctx.enter_context(nc.sbuf_tensor("c_iota_e", [P, E], I32))
        cleared = sem("c_cleared")
        counted = sem("c_counted")
        made = sem("c_made")
        block = ctx.enter_context(nc.Block())

        @block.gpsimd
        def _(pool):
            pool.memset(ident[:, :], 0.0).then_inc(cleared, 1)
            pool.memset(ident16[:, :], 0.0).then_inc(cleared, 1)
            pool.memset(strict[:, :], 1.0).then_inc(cleared, 1)
            pool.memset(ones16[:, :], 1.0).then_inc(made, 1)
            pool.iota(iota_i[:, :], [[0, 2], [1, E]], base=0, channel_multiplier=0).then_inc(counted, 1)
            pool.iota(iota_e[:, :], [[capacity, E]], base=0, channel_multiplier=0).then_inc(counted, 1)
            pool.iota(tok[:, :], [[P, 2]], base=0, channel_multiplier=1).then_inc(made, 1)
            pool.wait_ge(cleared, 3)
            for m in (ident, ident16):
                pool.affine_select(out=m[:, :], in_=m[:, :], compare_op=ALU.not_equal, fill=1.0, base=0,
                                   pattern=[[-1, P]], channel_multiplier=1).then_inc(made, 1)
            pool.affine_select(out=strict[:, :], in_=strict[:, :], compare_op=ALU.is_gt, fill=0.0, base=0,
                               pattern=[[1, P]], channel_multiplier=-1).then_inc(made, 1)

        @block.vector
        def _(dve):
            dve.wait_ge(counted, 2)
            dve.tensor_scalar(expert_order[:, :, :].rearrange("p a e -> p (a e)"), iota_i[:, :], -1.0, float(E),
                              ALU.mult, ALU.add).then_inc(made, 1)
            dve.tensor_copy(next_slot[:, :], iota_e[:, :]).then_inc(made, 1)


def attend(nc, x, ctx_in, x1, xn_parts, slots, router_parts, router_scale, ident, ident16, strict, ones16,
           expert_order, tok, next_slot):
    B, S, H = x.shape
    C = ctx_in.shape[2]
    E = expert_order.shape[2]
    HT = H // P
    NH = KV * G
    assert S == 2 * P and C == KV * D and H == NH * D and HT == 8
    LEAD, TAIL = 6, 4
    RSQRT = 12
    CHOSEN, COUNTS_READ, ROUTE = 14, 16, 24
    assert (B - LEAD) % 2 == 0 and B > LEAD + 2
    cap = slots.shape[0]

    with ExitStack() as ctx:
        def sb(name, shape, dt):
            return ctx.enter_context(nc.sbuf_tensor(name, shape, dt))

        def ps(name, shape, dt):
            return ctx.enter_context(nc.psum_tensor(name, shape, dt))

        def sem(name):
            return ctx.enter_context(nc.semaphore(name))

        xin = sb("a_x", [P, 2, H], F32)
        cin = sb("a_ctx", [P, 2, 2, C], F32)
        xn = sb("a_xn", [P, 2, H], F32)
        qsrc = sb("a_qsrc", [P, 2, 2, NH, P], F16)
        ksrc = sb("a_ksrc", [P, 2, KV, P], F16)
        QS = sb("a_qs", [P, 2, KV, G * S], F16)
        KS = sb("a_ks", [P, 2, KV, S], F16)
        V1 = sb("a_v", [P, 2, 2, KV, 2 * D], F32)
        PT = sb("a_p", [P, 4, 2, 2, 2 * S], F32)
        OS = sb("a_o", [P, 2, 2 * S], F32)
        att = sb("a_att", [P, 2, 4, 2, D], F32)
        xres = sb("a_xres", [P, 2, 2, H], F32)
        xn2 = sb("a_xn2", [P, 2, H], F32)
        xhl = sb("a_xhl", [P, 2, 2, 2 * H], F16)
        xT2 = sb("a_xt2", [P, 2, 2, HT, P], F16)
        st1, st2 = sb("a_st1", [P, 2, 2, 6], F32), sb("a_st2", [P, 2, 2, 6], F32)
        mv1, mv2 = sb("a_mv1", [P, 2, 2], F32), sb("a_mv2", [P, 2, 2], F32)
        veps, vysq, ysq = sb("a_veps", [P, 2, 2], F32), sb("a_vysq", [P, 2, 2], F32), sb("a_ysq", [P, 2, 2], F32)
        vhalf = sb("a_vhalf", [P, 2, 2], I32)
        rs1, rs2 = sb("a_rs1", [P, 2], F32), sb("a_rs2", [P, 2], F32)
        nb1, nb2 = sb("a_nb1", [P, 2], F32), sb("a_nb2", [P, 2], F32)
        cmax, call, cgrd = sb("a_cmax", [P, 1], F32), sb("a_call", [P, 1], F32), sb("a_cgrd", [P, 1], F32)
        cpow, crec, cinv = sb("a_cpow", [P, 1], F32), sb("a_crec", [P, 1], F32), sb("a_cinv", [P, 1], F32)
        escale = sb("a_escale", [P, 2], F32)
        nmax = sb("a_nmax", [P, 2, NH], F32)
        mhl = sb("a_mhl", [2 * G, 2, 2, S], F16)
        orec = sb("a_orec", [P, 2, 4, 2], F32)
        logit = sb("a_logit", [P, 2, E], F32)
        m1, m2 = sb("a_m1", [P, 2], F32), sb("a_m2", [P, 2], F32)
        eq, pri = sb("a_eq", [P, 2, E], F32), sb("a_pri", [P, 2, E], F32)
        pm = sb("a_pm", [P, 2], F32)
        pick = sb("a_pick", [P, 2, 2, E], F32)
        logit2 = sb("a_logit2", [P, 2, E], F32)
        both = sb("a_both", [P, 2, E], F16)
        diff, edge, den = sb("a_diff", [P, 2], F32), sb("a_edge", [P, 2], F32), sb("a_den", [P, 2], F32)
        pos = sb("a_pos", [P, 2, E], F32)
        posc = sb("a_posc", [P, 2, 2, E], F32)
        where = sb("a_where", [P, 2, 2], F32)
        slot_ix = sb("a_slot_ix", [P, 2, 2], U32)
        entry = sb("a_entry", [P, 2, 2, 2], U32)
        entry_f = entry[:, :, :, :].rearrange("p a b c -> p (a b c)").bitcast(F32)\
            .rearrange("p (a b c) -> p a b c", a=2, b=2)

        TR = ps("a_tr", [P, HT, P], F16)
        MX = ps("a_mx", [P, 2, 2, S], F32)
        SC = ps("a_sc", [P, 2, 2 * S], F32)
        PV = ps("a_pv", [P, 2 * S], F32)
        OT = ps("a_ot", [P, 4, P], F32)
        MI = ps("a_mi", [P, 512], F32)
        LG = MI[:, 256:256 + 2 * E].rearrange("p (c e) -> p c e", c=2)
        CN = MI[:, 320:320 + 3 * E].rearrange("p (c e) -> p c e", c=3)

        x_in = sem("x_in")
        ctx_got = [sem("ctx_in0"), sem("ctx_in1")]
        xres_in = [sem("xres_in0"), sem("xres_in1")]
        passed, sp_passed, dve_passed = sem("a_passed"), sem("a_sp_passed"), sem("a_dve_passed")
        filled = sem("a_filled")
        rows_cleared = sem("a_rows_cleared")
        n = {}
        for name in ("stats1", "aggr1", "rstd1", "nbias1", "xn_done", "q_high", "q_low", "q_high2",
                     "ctx_max", "ctx_all", "ctx_chain", "k_high", "k_low", "escaled", "v_made",
                     "q_turned", "q_there", "k_turned", "k_there", "max_scores", "maxed",
                     "max_turned", "max_high", "max_low", "scores", "exps", "pv", "o_there", "o_turned",
                     "o_recip", "o_done", "x1_done",
                     "stats2", "aggr2", "rstd2", "nbias2", "xn2_done", "x_high", "x_low",
                     "x2_turned", "x2_there", "logits", "route", "edged", "counts",
                     "x1_stored"):
            n[name] = sem("a_" + name)
        newt = [sem("a_newton1"), sem("a_newton2")]
        xn_stored = [sem("xn_stored0"), sem("xn_stored1")]
        max_in = [sem("max_in0"), sem("max_in1")]
        scattered = sem("scattered")
        block = ctx.enter_context(nc.Block())

        def over_batches(eng, body):
            for i in range(LEAD):
                body(i, i % 2)
            with eng.Fori(LEAD // 2, B // 2 - 1) as r:
                body(r * 2, 0)
                body(r * 2 + 1, 1)
            for i in range(B - 2, B + TAIL):
                body(i, i % 2)

        def on(b):
            return not isinstance(b, int) or 0 <= b < B

        def qt(i, k):
            return i - 1, k

        def mx(i, k):
            return (i - 1, k - 1) if k >= 1 else (i - 2, 7)

        def scu(i, k):
            return (i - 1, k - 5) if k >= 5 else (i - 2, k + 3)

        def pvu(i, k):
            return i - 2, k

        def otu(i, k):
            return (i - 2, k - 1) if k >= 1 else (i - 3, 7)

        def mtu(i, k):
            return (i - 1, k // 2 - 1) if k >= 2 else (i - 2, 3)

        def wait_par(eng, sems, b, par, each=16):
            eng.wait_ge(sems[par], (b - par) * (each // 2) + each)

        @block.sync
        def _(sp):
            xr = x.rearrange("b (c p) h -> b p c h", p=P)
            cr = ctx_in.rearrange("b (c p) h -> b p c h", p=P)

            def load_x(b):
                at_least(sp, n["xn_done"], b * 2)
                sp.dma_start(xin[:, :, :], xr[bass.ds(b, 1)].rearrange("a p c h -> (a p) c h")).then_inc(x_in, 16)

            def load_ctx(b, par):
                at_least(sp, n["v_made"], (b - 1) * 2)
                settle(sp, sp_passed)
                at_least(sp, n["k_low"], b - 1)
                sp.dma_start(cin[:, par, :, :], cr[bass.ds(b, 1)].rearrange("a p c h -> (a p) c h"))\
                    .then_inc(ctx_got[par], 16)

            def load_xres(b, par):
                at_least(sp, n["x1_stored"], (b - 1) * 16)
                settle(sp, sp_passed)
                at_least(sp, n["xn2_done"], (b - 1) * 2)
                sp.dma_start(xres[:, par, :, :], xr[bass.ds(b, 1)].rearrange("a p c h -> (a p) c h"))\
                    .then_inc(xres_in[par], 16)

            def max_rows(b, par, p):
                sp.wait_ge(n["max_low"], b * 4 + (p + 1))
                for s in range(2):
                    sp.dma_start(QS[96 + s:97 + s, par, 2 * p:2 * p + 2, :]
                                 .rearrange("o v (g s) -> o (v g) s", g=G),
                                 mhl[:, p % 2, s, :]).then_inc(max_in[p % 2], 16)

            load_x(0)
            load_ctx(0, 0)

            def iteration(i, par):
                for k in range(8):
                    b, p = mtu(i, k - 1)
                    if k % 2 == 1 and on(b):
                        max_rows(b, par if k == 1 else 1 - par, p)
                    if k == 2 and on(i - 3):
                        sp.wait_ge(n["x1_done"], (i - 3) * 16 + 16)
                        sp.dma_start(x1[bass.ds((i - 3) * S, S), :].rearrange("(c p) h -> p c h", p=P),
                                     xres[:, 1 - par, :, :]).then_inc(n["x1_stored"], 16)
                    if k == 3 and on(i + 1):
                        load_x(i + 1)
                    if k == 4 and on(i + 1):
                        load_ctx(i + 1, 1 - par)
                    if k == 6 and on(i - 1):
                        load_xres(i - 1, 1 - par)
                    if k == 7 and on(i - 3):
                        sp.wait_ge(n["x_low"], (i - 3) * 2 + 2)
                        sp.dma_start(xn_parts[bass.ds((i - 3) * S, S), :].rearrange("(c p) h -> p c h", p=P),
                                     xhl[:, 1 - par, :, :]).then_inc(xn_stored[1 - par], 16)

            over_batches(sp, iteration)
            sp.wait_ge(n["x1_stored"], 16 * B)
            for s in xn_stored:
                sp.wait_ge(s, 8 * B)

        @block.tensor
        def _(pe):
            pe.wait_ge(filled, 4)
            pe.wait_ge(rows_cleared, 1)

            def turned_out(i, k):
                b, p = mtu(i, k - 2 + k % 2)
                if on(b):
                    at_least(pe, n["max_low"], b * 4 + (p + 1))
                elif not isinstance(i, int) or i > B:
                    pe.wait_ge(n["max_low"], B * 4)

            def values(i, k, par, tt):
                b, u = pvu(i, k)
                if not on(b):
                    return
                p, h = u // 2, u % 2
                if tt == 0:
                    pe.wait_ge(n["exps"], b * 32 + 4 * (2 * p + 2))
                    pe.wait_ge(n["v_made"], b * 2 + 2)
                    at_least(pe, n["o_there"], b * 8 + u)
                for v in range(2):
                    kv = 2 * p + v
                    last = pe.matmul(PV[2 * D * v:2 * D * (v + 1), :], V1[:, par, tt, kv, :],
                                     PT[:, kv % 4, h, tt, :], start=tt == 0, stop=tt == 1)
                if tt == 1:
                    last.then_inc(n["pv"], 1)

            def score(i, k, par, q):
                b, kv = scu(i, k)
                if not on(b):
                    return
                sp_ = (1 - par) if k >= 5 else par
                half, tt = q // 2, q % 2
                if q == 0:
                    pe.wait_ge(max_in[(kv // 2) % 2], b * 64 + 32 * (kv // 4 + 1))
                at_least(pe, n["exps"], b * 32 + (4 * kv + q - 1))
                pe.matmul(SC[:, q % 2, :], KS[:, sp_, kv, tt * P:(tt + 1) * P],
                          QS[:, sp_, kv, half * 2 * S:(half + 1) * 2 * S],
                          start=True, stop=True).then_inc(n["scores"], 1)

            def max_score(i, k, par, q):
                b, kv = mx(i, k)
                if not on(b):
                    return
                mp = (1 - par) if k >= 1 else par
                half, gp = q // 2, q % 2
                if q == 0:
                    pe.wait_ge(n["q_there"], b * 8 + (kv + 1))
                    pe.wait_ge(n["k_there"], b * 2 + 2)
                at_least(pe, n["maxed"], b * 32 + (4 * kv + q - 1))
                for g2 in range(2):
                    g = 2 * gp + g2
                    last = pe.matmul(MX[:, q % 2, g2, :],
                                     QS[0:96, mp, kv, g * S + half * P:g * S + half * P + P],
                                     KS[0:96, mp, kv, :], start=True, stop=True)
                last.then_inc(n["max_scores"], 1)

            def turn_q(i, k, par):
                b, kv = qt(i, k)
                if not on(b):
                    return
                at_least(pe, n["q_low"], b * 2 + 2)
                at_least(pe, n["q_high2"], b * 2 + 2)
                at_least(pe, n["q_there"], b * 8 + kv)
                if k == 0:
                    pe.wait_ge(n["k_there"], b * 2 + 2)
                if k == 7 and on(i):
                    pe.wait_ge(n["k_there"], i * 2 + 1)
                if 1 <= k <= 4 and on(i - 4):
                    pe.wait_ge(n["x2_there"], (i - 4) * 4 + k)
                for g in range(G):
                    for c in range(2):
                        last = pe.transpose(TR[:, 2 * g + c, :], qsrc[:, 1 - par, c, kv * G + g, :], ident16[:, :])
                last.then_inc(n["q_turned"], 1)

            def turn_x_or_k(i, k, par):
                if k < 4 and on(i - 4):
                    b, c, part = i - 4, k // 2, k % 2
                    pe.wait_ge(n["x_low"], b * 2 + 2)
                    at_least(pe, n["q_there"], (i - 1) * 8 + (k + 1) if on(i - 1) else 8 * B)
                    at_least(pe, n["x2_there"], b * 4 + k)
                    for t in range(HT):
                        last = pe.transpose(TR[:, t, :], xhl[:, par, c, part * H + t * P:part * H + (t + 1) * P],
                                            ident16[:, :])
                    last.then_inc(n["x2_turned"], 1)
                if k >= 6 and on(i):
                    b, tt = i, k - 6
                    pe.wait_ge(n["k_low"], b + 1)
                    if on(i - 1):
                        at_least(pe, n["q_there"], (i - 1) * 8 + (k + 1))
                    at_least(pe, n["k_there"], b * 2 + tt)
                    for kv in range(KV):
                        last = pe.transpose(TR[:, kv, :], ksrc[:, tt, kv, :], ident16[:, :])
                    last.then_inc(n["k_turned"], 1)

            def turn_o(i, k):
                b, u = otu(i, k)
                if not on(b):
                    return
                pe.wait_ge(n["o_there"], b * 8 + (u + 1))
                at_least(pe, n["o_done"], b * 8 + u)
                for c in range(2):
                    for g in range(2):
                        last = pe.transpose(OT[:, 2 * c + g, :],
                                            OS[:, u % 2, g * S + c * P:g * S + c * P + P], ident[:, :])
                last.then_inc(n["o_turned"], 1)

            def turn_max(i, k):
                b, p = mtu(i, k - 1)
                if k % 2 == 0 or not on(b):
                    return
                pe.wait_ge(n["maxed"], b * 32 + 8 * (p + 1))
                at_least(pe, n["max_low"], b * 4 + p)
                if k == 1 and on(i - 5):
                    pe.wait_ge(n["route"], (i - 5) * ROUTE + COUNTS_READ)
                if k == 7 and on(i - 4):
                    pe.wait_ge(n["route"], (i - 4) * ROUTE + 1)
                for c in range(2):
                    last = pe.transpose(MI[0:2 * G, c * P:(c + 1) * P], nmax[:, c, 8 * p:8 * p + 8], ident[:, :])
                last.then_inc(n["max_turned"], 1)

            def router(i):
                b = i - 4
                if not on(b):
                    return
                pe.wait_ge(n["x2_there"], b * 4 + 4)
                turned_out(i, 6)
                at_least(pe, n["route"], b * ROUTE)
                for c in range(2):
                    for t in range(HT):
                        for px, pr in ((0, 0), (0, 1), (1, 0)):
                            last = pe.matmul(LG[:, c, :], xT2[:, c, px, t, :], router_parts[:, t, pr, :],
                                             start=t == 0 and px + pr == 0, stop=t == HT - 1 and px == 1)
                last.then_inc(n["logits"], 1)

            def count(i):
                b = i - 4
                if not on(b):
                    return
                turned_out(i, 7)
                pe.wait_ge(n["route"], b * ROUTE + CHOSEN)
                pe.matmul(CN[:, 0, :], strict[:, :], both[:, 0, :], start=True, stop=True)
                pe.matmul(CN[:, 1, :], strict[:, :], both[:, 1, :], start=True, stop=False)
                pe.matmul(CN[:, 1, :], ones16[:, :], both[:, 0, :], start=False, stop=True)
                pe.matmul(CN[:, 2, :], ones16[:, :], both[:, 0, :], start=True, stop=False)
                pe.matmul(CN[:, 2, :], ones16[:, :], both[:, 1, :], start=False, stop=True)\
                    .then_inc(n["counts"], 1)

            def iteration(i, par):
                for k in range(8):
                    score(i, k, par, 0)
                    values(i, k, par, 0)
                    turn_q(i, k, par)
                    max_score(i, k, par, 0)
                    score(i, k, par, 1)
                    max_score(i, k, par, 1)
                    turn_max(i, k)
                    turn_o(i, k)
                    score(i, k, par, 2)
                    if k == 6:
                        router(i)
                    values(i, k, par, 1)
                    score(i, k, par, 3)
                    max_score(i, k, par, 2)
                    max_score(i, k, par, 3)
                    turn_x_or_k(i, k, par)
                    if k == 7:
                        count(i)

            over_batches(pe, iteration)

        @block.scalar
        def _(act):
            act.wait_ge(filled, 4)

            def exps(i, k, par, q):
                b, kv = scu(i, k)
                if not on(b):
                    return
                sp_ = (1 - par) if k >= 5 else par
                h, tt = q // 2, q % 2
                if kv == 0 and q == 0:
                    act.wait_ge(n["escaled"], b + 1)
                act.wait_ge(n["scores"], b * 32 + (4 * kv + q + 1))
                at_least(act, n["pv"], b * 8 + (2 * (kv // 2) - 4 + h + 1))
                act.activation(PT[:, kv % 4, h, tt, :], SC[:, q % 2, :], ACT.Exp,
                               scale=escale[:, sp_:sp_ + 1]).then_inc(n["exps"], 1)

            def values_out(i, k):
                b, u = pvu(i, k)
                if on(b):
                    act.wait_ge(n["pv"], b * 8 + (u + 1))
                    at_least(act, n["o_turned"], b * 8 + (u - 1))
                    act.activation(OS[:, u % 2, :], PV[:, :], ACT.Copy).then_inc(n["o_there"], 1)

            def x_or_k_out(i, k, par):
                if k < 4 and on(i - 4):
                    b, c, part = i - 4, k // 2, k % 2
                    act.wait_ge(n["x2_turned"], b * 4 + (k + 1))
                    at_least(act, n["logits"], b)
                    act.activation(xT2[:, c, part, :, :], TR[:, :, :], ACT.Copy).then_inc(n["x2_there"], 1)
                if k >= 6 and on(i):
                    tt = k - 6
                    act.wait_ge(n["k_turned"], i * 2 + (tt + 1))
                    at_least(act, n["scores"], (i - 1) * 32)
                    act.activation(KS[:, par, :, tt * P:(tt + 1) * P], TR[:, :, :], ACT.Copy)\
                        .then_inc(n["k_there"], 1)

            def norm_x(b, c):
                if c == 0:
                    act.wait_ge(n["nbias1"], b + 1)
                    at_least(act, n["q_low"], b * 2)
                act.activation(xn[:, c, :], xin[:, c, :], ACT.Identity, bias=nb1[:, c:c + 1],
                               scale=rs1[:, c:c + 1]).then_inc(n["xn_done"], 1)

            def high_q(b, par, c):
                at_least(act, n["q_turned"], (b - 1) * 8)
                act.wait_ge(n["xn_done"], b * 2 + (c + 1))
                act.activation(qsrc[:, par, c, :, 0:D], xn[:, c, :].rearrange("p (h d) -> p h d", d=D),
                               ACT.Copy).then_inc(n["q_high"], 1)

            def high_k(b, par, s):
                if s == 0:
                    act.wait_ge(n["ctx_chain"], b * 4 + 4)
                    at_least(act, n["k_turned"], b * 2)
                for c in range(2):
                    act.activation(ksrc[:, c, :, s * D:(s + 1) * D],
                                   cin[:, par, c, :].rearrange("p (v d) -> p v d", d=D),
                                   ACT.Copy, scale=cinv[:, 0:1]).then_inc(n["k_high"], 1)

            def norm_x1(b, par, c):
                if c == 0:
                    act.wait_ge(n["nbias2"], b + 1)
                    at_least(act, n["x_low"], b * 2)
                act.activation(xn2[:, c, :], xres[:, par, c, :], ACT.Identity, bias=nb2[:, c:c + 1],
                               scale=rs2[:, c:c + 1]).then_inc(n["xn2_done"], 1)

            def high_x(b, par, c):
                at_least(act, xn_stored[par], (b - par) * 8)
                at_least(act, n["x2_turned"], (b - 1) * 4)
                act.wait_ge(n["xn2_done"], b * 2 + (c + 1))
                act.activation(xhl[:, par, c, 0:H], xn2[:, c, :], ACT.Copy).then_inc(n["x_high"], 1)

            def gates(b):
                act.wait_ge(n["route"], b * ROUTE + 13)
                act.activation(edge[:, :], diff[:, :], ACT.Exp).then_inc(n["edged"], 1)

            def iteration(i, par):
                for k in range(8):
                    exps(i, k, par, 0)
                    if on(i - 3) and k in (5, 6):
                        (norm_x1 if k == 5 else high_x)(i - 3, 1 - par, 1)
                    if on(i) and k == 2:
                        high_k(i, par, 1)
                    if on(i) and k in (3, 4):
                        norm_x(i, 1) if k == 3 else high_q(i, par, 1)
                    exps(i, k, par, 1)
                    exps(i, k, par, 2)
                    if on(i - 4) and k == 7:
                        gates(i - 4)
                    values_out(i, k)
                    x_or_k_out(i, k, par)
                    exps(i, k, par, 3)
                    if on(i) and k == 1:
                        high_k(i, par, 0)
                    if on(i) and k in (2, 3):
                        norm_x(i, 0) if k == 2 else high_q(i, par, 0)
                    if on(i - 3) and k in (4, 5):
                        (norm_x1 if k == 4 else high_x)(i - 3, 1 - par, 0)

            over_batches(act, iteration)

        @block.gpsimd
        def _(pool):
            pool.memset(qsrc[:, :, :, :, 3 * D:P], 0.0).then_inc(filled, 1)
            pool.memset(ksrc[:, :, :, 3 * D:3 * D + 2], 1.0).then_inc(filled, 1)
            pool.memset(ksrc[:, :, :, 3 * D + 2:P], 0.0).then_inc(filled, 1)
            pool.memset(V1[:, :, :, :, D:2 * D], 1.0).then_inc(filled, 1)

            def newton(sem_, b, y, w):
                done = b * RSQRT + 3
                for r in range(3):
                    pool.wait_ge(sem_, done + 3 * r)
                    pool.tensor_tensor(ysq[:, w, :], y[:, :], y[:, :], ALU.mult).then_inc(sem_, 1)
                    pool.wait_ge(sem_, done + 3 * r + 1)
                    pool.tensor_tensor(vysq[:, w, :], ysq[:, w, :], veps[:, w, :], ALU.mult).then_inc(sem_, 1)
                    pool.wait_ge(sem_, done + 3 * r + 2)
                    settle(pool, passed)
                    pool.tensor_scalar(ysq[:, w, :], vysq[:, w, :], -0.5, 1.5, ALU.mult, ALU.add)\
                        .then_inc(newt[w], 1)
                    pool.wait_ge(newt[w], b * 3 + (r + 1))
                    pool.tensor_tensor(y[:, :], y[:, :], ysq[:, w, :], ALU.mult).then_inc(sem_, 1)

            def iteration(i, par):
                for k in range(8):
                    if k == 1 and on(i):
                        newton(n["rstd1"], i, rs1, 0)
                    if k == 0 and on(i):
                        pool.wait_ge(n["ctx_max"], i + 1)
                        at_least(pool, n["ctx_chain"], i * 4)
                        settle(pool, passed)
                        pool.partition_all_reduce(call[:, :], cmax[:, :], P, RMAX).then_inc(n["ctx_all"], 1)
                    b, u = otu(i, k)
                    bp = par if k >= 1 else 1 - par
                    if on(b):
                        p, h = u // 2, u % 2
                        if u == 0:
                            wait_par(pool, xres_in, b, bp)
                        pool.wait_ge(n["o_done"], b * 8 + (u + 1))
                        for c in range(2):
                            to = xres[:, bp, c, p * 2 * P:(p + 1) * 2 * P]\
                                .rearrange("p (v g d) -> p g v d", v=2, g=G)[:, 2 * h:2 * h + 2, :, :]
                            pool.tensor_tensor(to, att[:, u % 2, 2 * c:2 * c + 2, :, :], to, ALU.add)\
                                .then_inc(n["x1_done"], 1)
                    if k == 3 and on(i - 3):
                        b = i - 3
                        newton(n["rstd2"], b, rs2, 1)
                    if k == 2 and on(i - 1):
                        b, bp = i - 1, 1 - par
                        wait_par(pool, ctx_got, b, bp)
                        at_least(pool, n["pv"], (b - 1) * 8)
                        settle(pool, passed)
                        for c in range(2):
                            pool.tensor_copy(V1[:, bp, c, :, 0:D],
                                             cin[:, bp, c, :].rearrange("p (v d) -> p v d", d=D))\
                                .then_inc(n["v_made"], 1)
                    if k in (4, 5) and on(i):
                        c = k - 4
                        pool.wait_ge(n["q_high"], i * 2 + (c + 1))
                        pool.tensor_tensor(qsrc[:, par, c, :, D:2 * D],
                                           xn[:, c, :].rearrange("p (h d) -> p h d", d=D),
                                           qsrc[:, par, c, :, 0:D], ALU.subtract).then_inc(n["q_low"], 1)
                    if k in (6, 7) and on(i - 3):
                        b, c = i - 3, k - 6
                        pool.wait_ge(n["x_high"], b * 2 + (c + 1))
                        pool.tensor_tensor(xhl[:, 1 - par, c, H:2 * H], xn2[:, c, :], xhl[:, 1 - par, c, 0:H],
                                           ALU.subtract).then_inc(n["x_low"], 1)
                    if k == 7 and on(i - 4):
                        b = i - 4
                        pool.wait_ge(n["route"], b * ROUTE + ROUTE)
                        settle(pool, passed)
                        for a in range(2):
                            for c in range(2):
                                pool.indirect_dma_start(
                                    out=slots[:, :], out_offset=bass.IndirectOffsetOnAxis(
                                        ap=slot_ix[:, a, c:c + 1], axis=0),
                                    in_=entry[:, a, c, :], in_offset=None).then_inc(scattered, 16)

            over_batches(pool, iteration)
            pool.wait_ge(scattered, 64 * B)

        @block.vector
        def _(dve):
            dve.memset(QS[96:P, :, :, :].rearrange("p a b c -> p (a b c)").bitcast(F32), 0.0).then_inc(rows_cleared, 1)
            dve.wait_ge(rows_cleared, 1)

            def bc(ap, size):
                return ap.unsqueeze(2).to_broadcast([P, 2, size])

            def estimate(sem_, b, mv, y, w):
                dve.tensor_scalar(veps[:, w, :], mv[:, :, 1], EPS, None, ALU.add).then_inc(sem_, 1)
                dve.wait_ge(sem_, b * RSQRT + 1)
                dve.tensor_single_scalar(vhalf[:, w, :], veps[:, w, :].bitcast(I32), 1, ALU.arith_shift_right)\
                    .then_inc(sem_, 1)
                dve.wait_ge(sem_, b * RSQRT + 2)
                dve.tensor_scalar(y[:, :].bitcast(I32), vhalf[:, w, :], -1.0, float(0x5F3759DF), ALU.mult, ALU.add)\
                    .then_inc(sem_, 1)

            class Steps:

                def __init__(self, b, done):
                    self.b, self.done = b, done

                def then(self, issue):
                    at_least(dve, n["route"], self.b * ROUTE + self.done)
                    issue().then_inc(n["route"], 1)
                    self.done += 1

            def choose(b, a):
                src, m = (logit, m1) if a == 0 else (logit2, m2)
                s = Steps(b, 7 * a)
                if a == 0:
                    dve.wait_ge(n["logits"], b + 1)
                    s.then(lambda: dve.tensor_scalar(logit[:, :, :], LG, router_scale[:, 0:1], None, ALU.mult))
                s.then(lambda: dve.reduce_max(m[:, :], src[:, :, :], AX.X))
                s.then(lambda: dve.tensor_tensor(eq[:, :, :], src[:, :, :], bc(m[:, :], E), ALU.is_ge))
                s.then(lambda: dve.tensor_tensor(pri[:, :, :], eq[:, :, :], expert_order[:, :, :], ALU.mult))
                s.then(lambda: dve.reduce_max(pm[:, :], pri[:, :, :], AX.X))
                s.then(lambda: dve.tensor_tensor(pick[:, a, :, :], pri[:, :, :], bc(pm[:, :], E), ALU.is_equal))
                if a == 0:
                    s.then(lambda: dve.scalar_tensor_tensor(
                        out=logit2[:, :, :], in0=pick[:, 0, :, :], scalar=-3.0e38, in1=logit[:, :, :],
                        op0=ALU.mult, op1=ALU.add))
                else:
                    at_least(dve, n["edged"], b)
                    s.then(lambda: dve.tensor_tensor(diff[:, :], m2[:, :], m1[:, :], ALU.subtract))
                    s.then(lambda: dve.tensor_tensor(both[:, :, :], pick[:, 0, :, :], pick[:, 1, :, :], ALU.add))

            def place(b):
                s = Steps(b, CHOSEN)
                dve.wait_ge(n["counts"], b + 1)
                s.then(lambda: dve.tensor_tensor(pos[:, :, :], CN[:, 0:2, :],
                                                 next_slot[:, :].unsqueeze(1).to_broadcast([P, 2, E]), ALU.add))
                s.then(lambda: dve.tensor_tensor(next_slot[:, :], next_slot[:, :], CN[:, 2, :], ALU.add))
                assert s.done == COUNTS_READ
                s.then(lambda: dve.tensor_tensor(posc[:, :, :, :], pick[:, :, :, :],
                                                 pos[:, :, :].unsqueeze(1).to_broadcast([P, 2, 2, E]), ALU.mult))
                s.then(lambda: dve.tensor_reduce(where[:, :, :], posc[:, :, :, :], AX.X, ALU.add))
                at_least(dve, scattered, b * 64)
                s.then(lambda: dve.tensor_copy(slot_ix[:, :, :], where[:, :, :]))
                dve.wait_ge(n["edged"], b + 1)
                s.then(lambda: dve.tensor_scalar(den[:, :], edge[:, :], 1.0, None, ALU.add))
                s.then(lambda: dve.reciprocal(entry_f[:, 0, :, 1], den[:, :]))
                s.then(lambda: dve.tensor_tensor(entry_f[:, 1, :, 1], edge[:, :], entry_f[:, 0, :, 1], ALU.mult))
                s.then(lambda: dve.tensor_copy(entry[:, :, :, 0], tok[:, :].unsqueeze(1).to_broadcast([P, 2, 2])))
                s.then(lambda: dve.tensor_scalar(tok[:, :], tok[:, :], float(S), None, ALU.add))
                assert s.done == ROUTE

            def max_out(i, k, qs):
                b, kv = mx(i, k)
                if on(b):
                    for q in qs:
                        half, gp = q // 2, q % 2
                        dve.wait_ge(n["max_scores"], b * 32 + (4 * kv + q + 1))
                        if q == 0:
                            at_least(dve, n["max_turned"], b * 4 + (kv // 2) - 3)
                        dve.reduce_max(nmax[:, half, kv * G + 2 * gp:kv * G + 2 * gp + 2], MX[:, q % 2, :, :],
                                       AX.X, negate=True).then_inc(n["maxed"], 1)

            def q_out(i, k, par):
                b, kv = qt(i, k)
                if on(b):
                    dve.wait_ge(n["q_turned"], b * 8 + (kv + 1))
                    at_least(dve, n["scores"], (b - 2) * 32 + 4 * (kv + 1))
                    at_least(dve, n["max_scores"], (b - 2) * 32 + 4 * (kv + 1))
                    dve.tensor_copy(QS[0:96, 1 - par, kv, :], TR[0:96, :, :].rearrange("p a b -> p (a b)"))\
                        .then_inc(n["q_there"], 1)

            def o_out(i, k):
                b, u = otu(i, k)
                if on(b):
                    dve.wait_ge(n["o_turned"], b * 8 + (u + 1))
                    at_least(dve, n["x1_done"], b * 16 + 2 * (u - 1))
                    ot = OT[:, :, :].rearrange("p q (v d) -> p q v d", v=2)
                    dve.reciprocal(orec[:, u % 2, :, :], ot[:, :, :, D]).then_inc(n["o_recip"], 1)
                    dve.wait_ge(n["o_recip"], b * 8 + (u + 1))
                    dve.tensor_tensor(att[:, u % 2, :, :, :], ot[:, :, :, 0:D],
                                      orec[:, u % 2, :, :].unsqueeze(3).to_broadcast([P, 4, 2, D]),
                                      ALU.mult).then_inc(n["o_done"], 1)

            def max_rows_out(i, k):
                b, p = mtu(i, k - 1)
                if k % 2 == 1 and on(b):
                    dve.wait_ge(n["max_turned"], b * 4 + (p + 1))
                    at_least(dve, max_in[p % 2], b * 64 + 32 * (p // 2))
                    dve.tensor_copy(mhl[:, p % 2, 0, :], MI[0:2 * G, 0:S]).then_inc(n["max_high"], 1)
                    dve.wait_ge(n["max_high"], b * 4 + (p + 1))
                    dve.tensor_tensor(mhl[:, p % 2, 1, :], MI[0:2 * G, 0:S], mhl[:, p % 2, 0, :],
                                      ALU.subtract).then_inc(n["max_low"], 1)

            def norms(i, k, par):
                if k in (0, 1) and on(i):
                    if k == 0:
                        dve.wait_ge(x_in, i * 16 + 16)
                        at_least(dve, n["aggr1"], i * 2)
                    for s in range(2):
                        last = dve.bn_stats(st1[:, k, s, :], xin[:, k, s * 512:(s + 1) * 512])
                    last.then_inc(n["stats1"], 1)
                if k == 0 and on(i):
                    wait_par(dve, ctx_got, i, par)
                    at_least(dve, n["ctx_all"], i)
                    dve.reduce_max(cmax[:, :], cin[:, par, :, :], AX.XY, apply_absolute_value=True)\
                        .then_inc(n["ctx_max"], 1)
                if k == 1 and on(i):
                    dve.wait_ge(n["stats1"], i * 2 + 2)
                    at_least(dve, n["rstd1"], i * RSQRT)
                    settle(dve, dve_passed)
                    for c in range(2):
                        dve.bn_aggr(mv1[:, c, :], st1[:, c, :, :].rearrange("p a b -> p (a b)"))\
                            .then_inc(n["aggr1"], 1)
                    dve.wait_ge(n["aggr1"], i * 2 + 2)
                    at_least(dve, n["xn_done"], i * 2)
                    estimate(n["rstd1"], i, mv1, rs1, 0)
                if k == 1 and on(i):
                    dve.wait_ge(n["ctx_all"], i + 1)
                    at_least(dve, n["k_low"], i)
                    dve.tensor_scalar(cgrd[:, :], call[:, :], 1e-30, None, ALU.max).then_inc(n["ctx_chain"], 1)
                    dve.wait_ge(n["ctx_chain"], i * 4 + 1)
                    dve.tensor_single_scalar(cpow[:, :].bitcast(I32), cgrd[:, :].bitcast(I32), EXPONENT,
                                             ALU.bitwise_and).then_inc(n["ctx_chain"], 1)
                    dve.wait_ge(n["ctx_chain"], i * 4 + 2)
                    dve.reciprocal(crec[:, :], cpow[:, :]).then_inc(n["ctx_chain"], 1)
                    dve.wait_ge(n["ctx_chain"], i * 4 + 3)
                    dve.tensor_scalar(cinv[:, :], crec[:, :], 8.0, None, ALU.mult).then_inc(n["ctx_chain"], 1)
                if k == 2 and on(i):
                    dve.wait_ge(n["rstd1"], i * RSQRT + RSQRT)
                    dve.scalar_tensor_tensor(out=nb1[:, :], in0=mv1[:, :, 0], scalar=-1.0, in1=rs1[:, :],
                                             op0=ALU.mult, op1=ALU.mult).then_inc(n["nbias1"], 1)
                if k in (4, 5) and on(i):
                    c = k - 4
                    dve.wait_ge(n["q_high"], i * 2 + (c + 1))
                    dve.tensor_copy(qsrc[:, par, c, :, 2 * D:3 * D], qsrc[:, par, c, :, 0:D])\
                        .then_inc(n["q_high2"], 1)
                if k == 3 and on(i):
                    dve.wait_ge(n["k_high"], i * 4 + 4)
                    for c in range(2):
                        last = dve.scalar_tensor_tensor(
                            out=ksrc[:, c, :, 2 * D:3 * D],
                            in0=cin[:, par, c, :].rearrange("p (v d) -> p v d", d=D),
                            scalar=cinv[:, 0:1], in1=ksrc[:, c, :, 0:D], op0=ALU.mult, op1=ALU.subtract)
                    last.then_inc(n["k_low"], 1)
                if k == 5 and on(i):
                    at_least(dve, n["exps"], (i - 1) * 32)
                    dve.tensor_scalar(escale[:, par:par + 1], cpow[:, :], 0.125 / float(D) ** 0.5, None,
                                      ALU.mult).then_inc(n["escaled"], 1)
                if k in (2, 3) and on(i - 3):
                    b, c = i - 3, k - 2
                    if c == 0:
                        dve.wait_ge(n["x1_done"], b * 16 + 16)
                        at_least(dve, n["aggr2"], b * 2)
                    for s in range(2):
                        last = dve.bn_stats(st2[:, c, s, :], xres[:, 1 - par, c, s * 512:(s + 1) * 512])
                    last.then_inc(n["stats2"], 1)
                if k == 3 and on(i - 3):
                    b = i - 3
                    dve.wait_ge(n["stats2"], b * 2 + 2)
                    at_least(dve, n["rstd2"], b * RSQRT)
                    settle(dve, dve_passed)
                    for c in range(2):
                        dve.bn_aggr(mv2[:, c, :], st2[:, c, :, :].rearrange("p a b -> p (a b)"))\
                            .then_inc(n["aggr2"], 1)
                    dve.wait_ge(n["aggr2"], b * 2 + 2)
                    at_least(dve, n["xn2_done"], b * 2)
                    estimate(n["rstd2"], b, mv2, rs2, 1)
                if k == 4 and on(i - 3):
                    b = i - 3
                    dve.wait_ge(n["rstd2"], b * RSQRT + RSQRT)
                    at_least(dve, n["xn2_done"], b * 2)
                    dve.scalar_tensor_tensor(out=nb2[:, :], in0=mv2[:, :, 0], scalar=-1.0, in1=rs2[:, :],
                                             op0=ALU.mult, op1=ALU.mult).then_inc(n["nbias2"], 1)

            def iteration(i, par):
                for k in range(8):
                    max_out(i, k, (0, 1))
                    q_out(i, k, par)
                    o_out(i, k)
                    max_rows_out(i, k)
                    norms(i, k, par)
                    if k == 6 and on(i - 4):
                        choose(i - 4, 0)
                        choose(i - 4, 1)
                    max_out(i, k, (2, 3))
                    if k == 7 and on(i - 4):
                        place(i - 4)

            over_batches(dve, iteration)


def schedule(nc, next_slot, table, half_table, capacity):
    E = next_slot.shape[1]
    n_blocks, n_halves = table.shape[1], half_table.shape[1]
    n_most = max(n_blocks, n_halves)
    with ExitStack() as ctx:
        def sb(name, shape, dt):
            return ctx.enter_context(nc.sbuf_tensor(name, shape, dt))

        def sem(name):
            return ctx.enter_context(nc.semaphore(name))

        first = sb("s_first", [P, E], F32)
        count = sb("s_count", [P, E], F32)
        count_i = sb("s_count_i", [P, E], I32)
        halves_i = sb("s_halves_i", [P, E], I32)
        pairs_i = sb("s_pairs_i", [P, E], I32)
        halves = sb("s_halves", [P, E], F32)
        pairs = sb("s_pairs", [P, E], F32)
        capped = sb("s_capped", [P, E + 1], F32)
        placed = sb("s_placed", [P, E], F32)
        left = sb("s_left", [P, E], F32)
        first_left = sb("s_first_left", [P, E], F32)
        ends = sb("s_ends", [P, E + 1], F32)
        num_i = sb("s_num_i", [P, n_most * E], I32)
        first_i = sb("s_first_i", [P, E], I32)
        num = sb("s_num", [P, n_most, E], F32)
        past = sb("s_past", [P, n_most, E + 1], F32)
        within = sb("s_within", [P, n_most, E], F32)
        offs = sb("s_offs", [P, n_most, E], F32)
        expert = sb("s_expert", [P, n_most], F32)
        slot = sb("s_slot", [P, n_most], F32)
        counted, chain = sem("s_counted"), sem("s_chain")
        block = ctx.enter_context(nc.Block())

        @block.gpsimd
        def _(pool):
            pool.iota(num_i[:, :], [[1, n_most], [0, E]], base=0, channel_multiplier=0).then_inc(counted, 1)
            pool.iota(first_i[:, :], [[capacity, E]], base=0, channel_multiplier=0).then_inc(counted, 1)

        @block.vector
        def _(dve):
            done = [0]

            def step(ins):
                done[0] += 1
                ins.then_inc(chain, 1)
                dve.wait_ge(chain, done[0])

            def lay_out(to, n, size, blocks, start):
                def over_experts(ap):
                    return ap.unsqueeze(1).to_broadcast([P, n, E])

                step(dve.memset(ends[:, 0:1], 0.0))
                for e in range(E):
                    step(dve.tensor_tensor(ends[:, e + 1:e + 2], ends[:, e:e + 1], blocks[:, e:e + 1], ALU.add))
                step(dve.memset(past[:, 0:n, 0:1], 1.0))
                step(dve.tensor_tensor(past[:, 0:n, 1:E + 1], num[:, 0:n, :], over_experts(ends[:, 1:E + 1]),
                                       ALU.is_ge))
                step(dve.tensor_reduce(expert[:, 0:n], past[:, 0:n, 1:E + 1], AX.X, ALU.add))
                step(dve.tensor_scalar(to[:, :, 0], expert[:, 0:n], float(E - 1), None, ALU.min))
                step(dve.tensor_tensor(offs[:, 0:n, :], num[:, 0:n, :], over_experts(ends[:, 0:E]), ALU.subtract))
                step(dve.tensor_scalar(offs[:, 0:n, :], offs[:, 0:n, :], float(size), None, ALU.mult))
                step(dve.tensor_tensor(offs[:, 0:n, :], offs[:, 0:n, :], over_experts(start[:, :]), ALU.add))
                step(dve.tensor_tensor(within[:, 0:n, :], past[:, 0:n, 0:E], past[:, 0:n, 1:E + 1], ALU.subtract))
                step(dve.tensor_tensor(offs[:, 0:n, :], offs[:, 0:n, :], within[:, 0:n, :], ALU.mult))
                step(dve.tensor_reduce(slot[:, 0:n], offs[:, 0:n, :], AX.X, ALU.add))
                step(dve.scalar_tensor_tensor(out=to[:, :, 1], in0=past[:, 0:n, E], scalar=float(E * capacity),
                                              in1=slot[:, 0:n], op0=ALU.mult, op1=ALU.add))

            dve.wait_ge(counted, 2)
            step(dve.tensor_copy(first[:, :], first_i[:, :]))
            step(dve.tensor_copy(num[:, :, :].rearrange("p b e -> p (b e)"), num_i[:, :]))
            step(dve.tensor_tensor(count[:, :], next_slot[:, :], first[:, :], ALU.subtract))
            step(dve.tensor_scalar(count_i[:, :], count[:, :], float(BLOCK // 2 - 1), None, ALU.add))
            step(dve.tensor_single_scalar(halves_i[:, :], count_i[:, :], (BLOCK // 2).bit_length() - 1,
                                          ALU.arith_shift_right))
            step(dve.tensor_single_scalar(pairs_i[:, :], halves_i[:, :], 1, ALU.arith_shift_right))
            step(dve.tensor_copy(halves[:, :], halves_i[:, :]))
            step(dve.tensor_copy(pairs[:, :], pairs_i[:, :]))
            lay_out(table, n_blocks, BLOCK, pairs, first)
            step(dve.tensor_scalar(capped[:, :], ends[:, :], float(n_blocks), None, ALU.min))
            step(dve.tensor_tensor(placed[:, :], capped[:, 1:E + 1], capped[:, 0:E], ALU.subtract))
            step(dve.scalar_tensor_tensor(out=left[:, :], in0=placed[:, :], scalar=-2.0, in1=halves[:, :],
                                          op0=ALU.mult, op1=ALU.add))
            step(dve.scalar_tensor_tensor(out=first_left[:, :], in0=placed[:, :], scalar=float(BLOCK),
                                          in1=first[:, :], op0=ALU.mult, op1=ALU.add))
            lay_out(half_table, n_halves, BLOCK // 2, left, first_left)


def run_experts(nc, stage, size, out, xn_parts, slots, table, w1_parts, w2_parts, scales, ident16,
                tokens, experts):
    H = out.shape[1]
    HT = H // P
    FT = w1_parts.shape[0] // (experts * P)
    IT = w2_parts.shape[0] // (experts * P)
    FULL = IT - 1
    HALF = P // 2
    n_blocks = table.shape[1]
    TT = size // P
    GR = 2 * TT

    with ExitStack() as ctx:
        def sb(name, shape, dt):
            return ctx.enter_context(nc.sbuf_tensor(name, shape, dt))

        def ps(name, shape, dt):
            return ctx.enter_context(nc.psum_tensor(name, shape, dt))

        sems = []

        def sem(name):
            sems.append(ctx.enter_context(nc.semaphore(name)))
            return sems[-1]

        w1b = sb(f"{stage}_w1", [P, FT, HT, 2, P], F16)
        w2b = sb(f"{stage}_w2", [P, IT, 2, H], F16)
        scl = sb(f"{stage}_scales", [P, 4], F32)
        idx_x = sb(f"{stage}_idx_x", [P, TT, 2], U32)
        idx_y = sb(f"{stage}_idx_y", [P, TT, 2], U32)
        xg = sb(f"{stage}_xg", [P, TT, 2 * H], F16)
        xT = sb(f"{stage}_xt", [P, 2, HT, size], F16)
        silu = sb(f"{stage}_silu", [P, 2, size], F32)
        up5 = sb(f"{stage}_up5", [HALF, size], F32)
        prod = sb(f"{stage}_prod", [P, 2, size], F32)
        yT = sb(f"{stage}_yt", [P, 2, IT, size], F16)
        gate = sb(f"{stage}_gate", [P, TT], F32)
        rows = sb(f"{stage}_rows", [P, TT, H], F32)
        y1 = ps(f"{stage}_y1", [P, 4, 512], F32)[:, :, 0:size]
        y2 = ps(f"{stage}_y2", [P, 2, H // 2], F32)
        tr = ps(f"{stage}_tr", [P, 2, HT, P], F16)

        w1_in = [sem(f"{stage}_w1_in{j}") for j in range(FT)]
        w2_in = [sem(f"{stage}_w2_in{m}") for m in range(IT)]
        scl_in = sem(f"{stage}_scl_in")
        idx_x_in = sem(f"{stage}_idx_x_in")
        idx_y_in = sem(f"{stage}_idx_y_in")
        x_in = [sem(f"{stage}_x_in{c}") for c in range(TT)]
        rows_in = [sem(f"{stage}_rows_in{c}") for c in range(TT)]
        passed = sem(f"{stage}_passed")
        cleared = sem(f"{stage}_cleared")
        turned, x_there = sem(f"{stage}_turned"), sem(f"{stage}_x_there")
        y1_there = sem(f"{stage}_y1_there")
        silu_done, prod_done, high, low = sem(f"{stage}_silu_done"), sem(f"{stage}_prod_done"), sem(f"{stage}_high"), sem(f"{stage}_low")
        gates = sem(f"{stage}_gates")
        y2_there, added = sem(f"{stage}_y2_there"), sem(f"{stage}_added")
        rows_out = sem(f"{stage}_rows_out")
        with nc.Block() as clearing:
            @clearing.gpsimd
            def _(pool):
                for s in sems:
                    pool.sem_clear(s)

        block = ctx.enter_context(nc.Block())
        last_block = n_blocks - 1

        def over_blocks(eng, body):
            body(0)
            with eng.Fori(1, last_block) as i:
                body(i)
            body(last_block)

        def more(i):
            return not isinstance(i, int) or i < last_block

        @block.sync
        def _(sp):
            def where(i):
                e = sp.value_load(table[0:1, bass.ds(i, 1), 0:1], min_val=0, max_val=experts - 1)
                s = sp.value_load(table[0:1, bass.ds(i, 1), 1:2], min_val=0, max_val=slots.shape[0] - size)
                return e, s

            def load_slots(to, sem_, s):
                sp.dma_start(to[:, :, :], slots[bass.ds(s, size), :].rearrange("(p c) t -> p c t", p=P))\
                    .then_inc(sem_, 16)

            def load_w1(j, e):
                sp.dma_start(w1b[:, j, :, :, :].rearrange("p a b c -> p (a b c)"),
                             w1_parts[bass.ds(e * (FT * P) + j * P, P), :]).then_inc(w1_in[j], 16)

            def load_w2(m, e):
                sp.dma_start(w2b[:, m, :, :].rearrange("p a b -> p (a b)"),
                             w2_parts[bass.ds(e * (IT * P) + m * P, P), :]).then_inc(w2_in[m], 16)

            def load_scales(e):
                sp.dma_start(scl[:, :], scales[bass.ds(e * P, P), :]).then_inc(scl_in, 16)

            e, s = where(0)
            load_slots(idx_x, idx_x_in, s)
            load_scales(e)
            load_w1(0, e)
            for c in range(TT):
                sp.wait_ge(x_in[c], 16)
            for j in range(1, FT):
                load_w1(j, e)
            for m in range(IT):
                load_w2(m, e)

            def one(i):
                _, s0 = where(i)
                if more(i):
                    e, s = where(i + 1)
                    for c in range(TT):
                        sp.wait_ge(x_in[c], i * 16 + 16)
                    load_slots(idx_x, idx_x_in, s)
                at_least(sp, rows_out, i * (16 * TT))
                at_least(sp, gates, i)
                load_slots(idx_y, idx_y_in, s0)
                if more(i):
                    for j in range(FT):
                        sp.wait_ge(y1_there, i * FT + (j + 1))
                        load_w1(j, e)
                    sp.wait_ge(silu_done, i * IT + IT)
                    sp.wait_ge(prod_done, i * IT + IT)
                    sp.wait_ge(gates, i + 1)
                    load_scales(e)
                    sp.wait_ge(y2_there, i * GR + GR)
                    for m in range(IT):
                        load_w2(m, e)

            over_blocks(sp, one)

        @block.gpsimd
        def _(pool):
            pool.memset(xg[:, :, :].rearrange("p a b -> p (a b)").bitcast(U32), 0).then_inc(cleared, 1)
            pool.memset(rows[:, :, :], 0.0).then_inc(cleared, 1)
            pool.wait_ge(cleared, 2)

            def gather_x():
                for c in range(TT):
                    pool.indirect_dma_start(
                        out=xg[:, c, :], out_offset=None, in_=xn_parts[:, :],
                        in_offset=bass.IndirectOffsetOnAxis(ap=idx_x[:, c, 0:1], axis=0),
                        bounds_check=tokens - 1, oob_is_err=False).then_inc(x_in[c], 16)

            pool.wait_ge(idx_x_in, 16)
            gather_x()

            def one(i):
                if more(i):
                    pool.wait_ge(idx_x_in, i * 16 + 32)
                    pool.wait_ge(turned, i * GR + GR)
                    settle(pool, passed)
                    gather_x()
                pool.wait_ge(idx_y_in, i * 16 + 16)
                settle(pool, passed)
                for c in range(TT):
                    pool.indirect_dma_start(
                        out=rows[:, c, :], out_offset=None, in_=out[:, :],
                        in_offset=bass.IndirectOffsetOnAxis(ap=idx_y[:, c, 0:1], axis=0),
                        bounds_check=tokens - 1, oob_is_err=False).then_inc(rows_in[c], 16)
                for c in range(TT):
                    pool.wait_ge(added, i * GR + 2 * (c + 1))
                    settle(pool, passed)
                    pool.indirect_dma_start(
                        out=out[:, :], out_offset=bass.IndirectOffsetOnAxis(ap=idx_y[:, c, 0:1], axis=0),
                        in_=rows[:, c, :], in_offset=None,
                        bounds_check=tokens - 1, oob_is_err=False).then_inc(rows_out, 16)

            over_blocks(pool, one)
            pool.wait_ge(rows_out, n_blocks * 16 * TT)

        def turn(pe, b, g):
            c, part = g // 2, g % 2
            pe.wait_ge(x_in[c], b * 16 + 16)
            at_least(pe, x_there, b * GR + (g - 1))
            for t in range(HT):
                last = pe.transpose(tr[:, g % 2, t, :], xg[:, c, part * H + t * P:part * H + (t + 1) * P],
                                    ident16[:, :])
            last.then_inc(turned, 1)

        @block.tensor
        def _(pe):
            pe.wait_ge(cleared, 2)
            for g in range(GR):
                turn(pe, 0, g)

            def one(i):
                pe.wait_ge(x_there, i * GR + GR)
                for j in range(FT):
                    m, up = j // 2, j % 2
                    bank = 2 * (m % 2) + up
                    pe.wait_ge(w1_in[j], i * 16 + 16)
                    at_least(pe, prod_done if up else silu_done, i * IT + (m - 1))
                    n = 0
                    for t in range(HT):
                        for pw, px in ((0, 0), (0, 1), (1, 0)):
                            last = pe.matmul(y1[:, bank, :], w1b[:, j, t, pw, :], xT[:, px, t, :],
                                             start=n == 0, stop=n == 3 * HT - 1)
                            n += 1
                    last.then_inc(y1_there, 1)
                for g in range(GR):
                    if more(i):
                        turn(pe, i + 1, g)
                    c, half = g // 2, g % 2
                    at_least(pe, added, i * GR + (g - 1))
                    cols = slice(c * P, (c + 1) * P)
                    outs = slice(half * (H // 2), (half + 1) * (H // 2))
                    for m in range(IT):
                        if g == 0:
                            pe.wait_ge(w2_in[m], i * 16 + 16)
                            pe.wait_ge(low, i * IT + (m + 1))
                        terms = ((0, 0), (0, 1), (1, 0)) if m < FULL else ((0, 0), (0, 1))
                        for py, pw in terms:
                            last = pe.matmul(y2[:, g % 2, :], yT[:, py, m, cols], w2b[:, m, pw, outs],
                                             start=m == 0 and py + pw == 0, stop=m == FULL and pw == 1)
                    last.then_inc(y2_there, 1)

            over_blocks(pe, one)

        @block.scalar
        def _(act):
            def high_of(i, m):
                act.wait_ge(prod_done, i * IT + (m + 1))
                if m == 0:
                    at_least(act, y2_there, i * GR)
                rows_of = P if m < FULL else HALF
                act.activation(yT[0:rows_of, 0, m, :], prod[0:rows_of, m % 2, :], ACT.Copy).then_inc(high, 1)

            def one(i):
                act.wait_ge(scl_in, i * 16 + 16)
                for m in range(IT):
                    at_least(act, prod_done, i * IT + (m - 1))
                    act.wait_ge(y1_there, i * FT + (2 * m + 1))
                    bank = 2 * (m % 2)
                    if m < FULL:
                        act.activation(silu[:, m % 2, :], y1[:, bank, :], ACT.Silu, scale=scl[:, 0:1])\
                            .then_inc(silu_done, 1)
                    else:
                        act.activation(silu[0:HALF, m % 2, :], y1[0:HALF, bank, :], ACT.Silu,
                                       scale=scl[0:HALF, 0:1])
                        act.activation(up5[:, :], y1[HALF:P, bank, :], ACT.Copy, scale=scl[HALF:P, 1:2])\
                            .then_inc(silu_done, 1)
                    if m >= 1:
                        high_of(i, m - 1)
                high_of(i, FULL)

            over_blocks(act, one)

        @block.vector
        def _(dve):
            def turn_out(b, g):
                c, part = g // 2, g % 2
                dve.wait_ge(turned, b * GR + (g + 1))
                dve.tensor_copy(xT[:, part, :, c * P:(c + 1) * P], tr[:, g % 2, :, :]).then_inc(x_there, 1)

            for g in range(GR):
                turn_out(0, g)

            def low_of(i, m):
                dve.wait_ge(high, i * IT + (m + 1))
                if m < FULL:
                    to, part, src = yT[:, 1, m, :], yT[:, 0, m, :], prod[:, m % 2, :]
                else:
                    to, part, src = yT[HALF:P, 0, m, :], yT[0:HALF, 0, m, :], prod[0:HALF, m % 2, :]
                dve.tensor_tensor(to, src, part, ALU.subtract).then_inc(low, 1)

            def one(i):
                dve.wait_ge(idx_y_in, i * 16 + 16)
                dve.wait_ge(scl_in, i * 16 + 16)
                at_least(dve, added, i * GR)
                dve.tensor_scalar(gate[:, :], idx_y[:, :, 1].bitcast(F32), scl[:, 2:3], None, ALU.mult)\
                    .then_inc(gates, 1)
                for m in range(IT):
                    dve.wait_ge(silu_done, i * IT + (m + 1))
                    at_least(dve, low, i * IT + (m - 1))
                    if m < FULL:
                        dve.wait_ge(y1_there, i * FT + (2 * m + 2))
                        dve.scalar_tensor_tensor(out=prod[:, m % 2, :], in0=y1[:, 2 * (m % 2) + 1, :],
                                                 scalar=scl[:, 1:2], in1=silu[:, m % 2, :],
                                                 op0=ALU.mult, op1=ALU.mult).then_inc(prod_done, 1)
                    else:
                        dve.tensor_tensor(prod[0:HALF, m % 2, :], up5[:, :], silu[0:HALF, m % 2, :], ALU.mult)\
                            .then_inc(prod_done, 1)
                    if m >= 1:
                        low_of(i, m - 1)
                low_of(i, FULL)
                dve.wait_ge(gates, i + 1)
                for g in range(GR):
                    c, half = g // 2, g % 2
                    outs = slice(half * (H // 2), (half + 1) * (H // 2))
                    if more(i):
                        turn_out(i + 1, g)
                    dve.wait_ge(y2_there, i * GR + (g + 1))
                    if half == 0:
                        dve.wait_ge(rows_in[c], i * 16 + 16)
                    dve.scalar_tensor_tensor(out=rows[:, c, outs], in0=y2[:, g % 2, :], scalar=gate[:, c:c + 1],
                                             in1=rows[:, c, outs], op0=ALU.mult, op1=ALU.add).then_inc(added, 1)

            over_blocks(dve, one)


def attention_and_experts(nc, x, ctx_in, router_w, w1, w2, out):
    B, S, H = x.shape
    E, F2, _ = w1.shape
    I = F2 // 2
    T = B * S
    capacity = T + BLOCK
    most_halves = (2 * T - E) // (BLOCK // 2) + E
    n_blocks = (most_halves - (E - 1)) // 2
    n_halves = max(E, most_halves - 2 * n_blocks)
    FT, IT = F2 // P, -(-I // P)
    out_rows = out.rearrange("b s h -> (b s) h")

    def scratch(name, shape, dt):
        return nc.dram_tensor(name, shape, dt, kind="Internal").ap()

    w1_parts = scratch("w1_parts", (E * FT * P, 2 * H), F16)
    w2_parts = scratch("w2_parts", (E * IT * P, 2 * H), F16)
    scales = scratch("scales", (E * P, 4), F32)
    xn_parts = scratch("xn_parts", (T, 2 * H), F16)
    slots = scratch("slots", (E * capacity + BLOCK, 2), U32)

    with ExitStack() as ctx:
        def sb(name, shape, dt):
            return ctx.enter_context(nc.sbuf_tensor(name, shape, dt))

        ident = sb("ident", [P, P], F32)
        ident16 = sb("ident16", [P, P], F16)
        strict = sb("strict", [P, P], F16)
        ones16 = sb("ones16", [P, P], F16)
        expert_order = sb("expert_order", [P, 2, E], F32)
        tok = sb("tok", [P, 2], U32)
        next_slot = sb("next_slot", [P, E], F32)
        router_parts = sb("router_parts", [P, H // P, 2, E], F16)
        router_scale = sb("router_scale", [P, 1], F32)
        table = sb("table", [P, n_blocks, 2], I32)
        half_table = sb("half_table", [P, n_halves, 2], I32)

        make_constants(nc, ident, ident16, strict, ones16, expert_order, tok, next_slot, capacity)
        prepare_weights(nc, w1, w2, router_w, w1_parts, w2_parts, scales, slots, router_parts, router_scale,
                        ident, T)
        attend(nc, x, ctx_in, out_rows, xn_parts, slots, router_parts, router_scale, ident, ident16, strict,
               ones16, expert_order, tok, next_slot)
        schedule(nc, next_slot, table, half_table, capacity)
        run_experts(nc, "f", BLOCK, out_rows, xn_parts, slots, table, w1_parts, w2_parts, scales, ident16, T, E)
        run_experts(nc, "h", BLOCK // 2, out_rows, xn_parts, slots, half_table, w1_parts, w2_parts, scales,
                    ident16, T, E)


def kernel(x, ctx_512, L0_ffn_router_w, L0_ffn_w1, L0_ffn_w2):
    import numpy as np
    import concourse.bacc as bacc
    from concourse.bass_utils import run_bass_kernel_spmd

    nc = bacc.Bacc("TRN2", target_bir_lowering=False, num_devices=1)
    arrays, aps = {}, []
    for name, a in (("x", x), ("ctx_512", ctx_512), ("router_w", L0_ffn_router_w), ("w1", L0_ffn_w1),
                    ("w2", L0_ffn_w2)):
        a = np.ascontiguousarray(a)
        arrays[f"in_{name}"] = a
        aps.append(nc.dram_tensor(f"in_{name}", a.shape, mybir.dt.from_np(a.dtype), kind="ExternalInput").ap())
    out = nc.dram_tensor("out", arrays["in_x"].shape, F32, kind="ExternalOutput").ap()
    attention_and_experts(nc, *aps, out)
    result = run_bass_kernel_spmd(nc, [arrays], core_ids=[0])
    return result.results[0]["out"]
```
